# Optimizing a Trainium2 kernel written in Bass

```python
import numpy as np
import jax
import jax.numpy as jnp

def _softmax(x, axis=-1):
    return jax.nn.softmax(x, axis=axis)

def _gelu(x):
    return jax.nn.gelu(x, approximate=True)

def _silu(x):
    return jax.nn.silu(x)

def _sigmoid(x):
    return jax.nn.sigmoid(x)

def _layernorm(x, axis=-1, eps=1e-05):
    m = jnp.mean(x, axis=axis, keepdims=True)
    v = jnp.var(x, axis=axis, keepdims=True)
    return (x - m) / jnp.sqrt(v + eps)

def _scatter_add(tgt, idx, src, axis=0):
    return tgt.at[idx].add(src)

def _segment_sum(src, seg, n):
    return jax.ops.segment_sum(src, seg, n)
kernel_name = 'mk_gnn_preln_d1_gnn_r32_c167e8'

def setup_inputs(seed: int=0):
    np.random.seed(seed)
    _w = jnp.asarray

    def _rec_inputs():
        import jax
        import jax.numpy as jnp
        _gk = jax.random.key(seed)
        x = -0.0003713 + 1 * jax.random.normal(jax.random.fold_in(_gk, 1), (6250, 64), jnp.float32)
        src = jax.random.randint(jax.random.fold_in(_gk, 2), (200000,), 0, 6250, jnp.int32)
        dst = jnp.minimum((6250 * jax.random.uniform(jax.random.fold_in(_gk, 3), (200000,)) ** 2.0).astype(jnp.int32), 199999)
        _o = jnp.argsort(dst, stable=True)
        src = src[_o]
        dst = dst[_o]
        edge_attr_8 = 0.000196303 + 1.00016 * jax.random.normal(jax.random.fold_in(_gk, 11), (200000, 8), jnp.float32)
        return (x, src, dst, edge_attr_8)
    x, src, dst, edge_attr_8 = _rec_inputs()

    def _L0_gnn_setup():
        import jax, jax.numpy as jnp
        import numpy as np
        E = 6250
        M = 100000
        IN_DIM = 64
        EMBED = 64
        H = 8
        D = EMBED // H

        def _segment_softmax(logits, index, num_segments):
            seg_max = jax.ops.segment_max(logits, index, num_segments=num_segments)
            seg_max = jnp.where(jnp.isfinite(seg_max), seg_max, 0.0)
            ex = jnp.exp(logits - seg_max[index])
            seg_sum = jax.ops.segment_sum(ex, index, num_segments=num_segments)
            return ex / (seg_sum[index] + 1e-16)
        key = jax.random.key(seed)
        ks = jax.random.split(key, 12)
        s = 1.0 / np.sqrt(IN_DIM)
        inp = {'edge_features': jax.random.normal(ks[0], (E, IN_DIM), dtype=jnp.float32), 'e2e': jax.random.randint(ks[1], (2, M), 0, E, dtype=jnp.int32), 'attn_bias': jax.random.normal(ks[2], (M, H), dtype=jnp.float32), 'Wq': jax.random.uniform(ks[3], (IN_DIM, EMBED), jnp.float32, -s, s), 'bq': jax.random.uniform(ks[4], (EMBED,), jnp.float32, -s, s), 'Wk': jax.random.uniform(ks[5], (IN_DIM, EMBED), jnp.float32, -s, s), 'bk': jax.random.uniform(ks[6], (EMBED,), jnp.float32, -s, s), 'Wv': jax.random.uniform(ks[7], (IN_DIM, EMBED), jnp.float32, -s, s), 'bv': jax.random.uniform(ks[8], (EMBED,), jnp.float32, -s, s), 'Wo': jax.random.uniform(ks[9], (EMBED, EMBED), jnp.float32, -s, s), 'bo': jax.random.uniform(ks[10], (EMBED,), jnp.float32, -s, s)}
        return inp
    _L0_gnn_all = _L0_gnn_setup()
    _L0_gnn_in = {k: v for k, v in _L0_gnn_all.items() if k in ('Wq', 'bq', 'Wk', 'bk', 'Wv', 'bv', 'Wo', 'bo')}
    del _L0_gnn_all
    return {'x': x, 'src': src, 'dst': dst, 'edge_attr_8': edge_attr_8, 'L0_gnn_Wq': _L0_gnn_in['Wq'], 'L0_gnn_bq': _L0_gnn_in['bq'], 'L0_gnn_Wk': _L0_gnn_in['Wk'], 'L0_gnn_bk': _L0_gnn_in['bk'], 'L0_gnn_Wv': _L0_gnn_in['Wv'], 'L0_gnn_bv': _L0_gnn_in['bv'], 'L0_gnn_Wo': _L0_gnn_in['Wo'], 'L0_gnn_bo': _L0_gnn_in['bo']}

def reference(x, src, dst, edge_attr_8, L0_gnn_Wq, L0_gnn_bq, L0_gnn_Wk, L0_gnn_bk, L0_gnn_Wv, L0_gnn_bv, L0_gnn_Wo, L0_gnn_bo):
    import jax
    import jax.numpy as jnp

    def _L0_gnn_ref(edge_features, e2e, attn_bias, Wq, bq, Wk, bk, Wv, bv, Wo, bo):
        import jax, jax.numpy as jnp
        import numpy as np
        E = 6250
        M = 100000
        IN_DIM = 64
        EMBED = 64
        H = 8
        D = EMBED // H

        def _segment_softmax(logits, index, num_segments):
            seg_max = jax.ops.segment_max(logits, index, num_segments=num_segments)
            seg_max = jnp.where(jnp.isfinite(seg_max), seg_max, 0.0)
            ex = jnp.exp(logits - seg_max[index])
            seg_sum = jax.ops.segment_sum(ex, index, num_segments=num_segments)
            return ex / (seg_sum[index] + 1e-16)
        src_e, dst_e = (e2e[0], e2e[1])
        scale = D ** (-0.5)
        q = (edge_features @ Wq + bq).reshape(E, H, D)
        k = (edge_features @ Wk + bk).reshape(E, H, D)
        v = (edge_features @ Wv + bv).reshape(E, H, D)
        q_dst = q[dst_e]
        k_src = k[src_e]
        logits = jnp.sum(q_dst * k_src, axis=-1) * scale
        logits = logits + attn_bias
        attn = _segment_softmax(logits, dst_e, E)
        msg = v[src_e] * attn[..., None]
        out = jax.ops.segment_sum(msg, dst_e, num_segments=E)
        out = out.reshape(E, EMBED)
        return out @ Wo + bo
    edge_index = jnp.stack([src, dst])
    h = jnp.maximum(_layernorm(x, axis=-1), 0.0)
    x = x + _L0_gnn_ref(h, edge_index, edge_attr_8, L0_gnn_Wq, L0_gnn_bq, L0_gnn_Wk, L0_gnn_bk, L0_gnn_Wv, L0_gnn_bv, L0_gnn_Wo, L0_gnn_bo)
    return x

_drawn_inputs = setup_inputs


def setup_inputs(seed=0):
    import zlib

    import numpy as np

    out = dict(_drawn_inputs(seed))
    spreads = {}
    factors = {'L0_gnn_Wq': 7.573, 'L0_gnn_bq': 8.0, 'L0_gnn_Wk': 7.1, 'L0_gnn_bk': 8.0}
    for name, (base, spread) in spreads.items():
        noise = np.random.default_rng([zlib.crc32(name.encode()), seed]).standard_normal(out[name].shape)
        drawn = base * np.exp(spread * noise) if base else spread * noise
        out[name] = jnp.asarray(drawn.astype(out[name].dtype))
    for name, factor in factors.items():
        out[name] = (out[name] * factor).astype(out[name].dtype)
    return out
```

```python
from contextlib import ExitStack

import numpy as np
import concourse.bass as bass
from concourse import mybir

ALU = mybir.AluOpType
ACT = mybir.ActivationFunctionType
AX_X = mybir.AxisListType.X
F32 = mybir.dt.float32
BF16 = mybir.dt.bfloat16
I32 = mybir.dt.int32

P = 128
N, F = 6250, 64
E = 200000
H, D = 8, 8
NB = 52
NCH = 4
CH = NB // NCH
FULLB, TAILN = N // P, N % P
SLOTS = 8
GE = P * SLOTS
GC = 7
NG = -(-E // GE)
NS = NG // GC
TAILE = E - (NG - 1) * GE
TAILP = TAILE // SLOTS
SE = GC * GE
ROWS = GC * H
MAXPAIRS = (GC + FULLB + 1) // 2
KT = 2 * (MAXPAIRS + 1)
AW = H * (D + 1)
WW = AW + H
BIG = 3.0e38
NODST = 30000
SCALE = float(D) ** -0.5
assert NS * GC == NG and NS % 2 == 0 and TAILE % SLOTS == 0 and E % SLOTS == 0


def build(nc, x, src, dst, attr, Wq, bq, Wk, bk, Wv, bv, Wo, bo, out):
    kv_dram = nc.dram_tensor("kv_table", [NB * P, 2 * F], F32, kind="Internal").ap()
    group_dram = nc.dram_tensor("group_table", [NS, KT], I32, kind="Internal").ap()
    base_dram = nc.dram_tensor("base_table", [NS, KT], F32, kind="Internal").ap()
    meta_dram = nc.dram_tensor("meta_table", [2, NS], F32, kind="Internal").ap()

    with ExitStack() as ctx:
        def sb(name, shape, dt=F32):
            return ctx.enter_context(nc.sbuf_tensor(name, shape, dt))

        def ps(name, shape, dt=F32):
            return ctx.enter_context(nc.psum_tensor(name, shape, dt))

        def sem(name):
            return ctx.enter_context(nc.semaphore(name))

        ident = sb("ident", [P, P])
        ident_bf = sb("ident_bf", [P, P], BF16)
        iota_i = sb("iota_i", [P, P], I32)
        iota = sb("iota", [P, P])
        iota_bf = sb("iota_bf", [P, P], BF16)
        xs = sb("xs", [P, NB, F])
        nodes = sb("nodes", [P, NB, F])
        work = sb("work", [P, NB, F])
        stat = sb("stat", [P, 4, NB])
        nodesT = sb("nodesT", [F + 1, 2, P])
        wqkv = sb("wqkv", [F + 1, 3 * F])
        wo = sb("wo", [F + 1, F])
        q_parts = sb("q_parts", [P, 3, NB, F], BF16)
        dst_i = sb("dst_i", [P, NG * SLOTS], I32)
        last_dst = sb("last_dst", [NS, GC], I32)
        first_dst = sb("first_dst", [NS, 1], I32)
        last_blk = sb("last_blk", [NS, GC], I32)
        first_blk = sb("first_blk", [NS, 1], I32)
        first_f = sb("first_f", [NS, 1])
        last_step = sb("last_step", [NS, GC])
        reach = sb("reach", [NS, KT, GC])
        tab = sb("tab", [NS, 2, KT])
        tab_g = sb("tab_g", [NS, KT], I32)
        meta = sb("meta", [NS, 2])
        iti = sb("iti", [NS, 2], I32)
        meta_row = sb("meta_row", [1, 2, NS])
        first_row = sb("first_row", [1, NS], I32)
        base128 = sb("base128", [P, NS * KT])
        steps = sb("steps", [1, NS * KT], I32)
        pairs = sb("pairs", [1, NS], I32)
        begin_f = sb("begin_f", [1, NS + 1])
        begin = sb("begin", [1, NS + 1], I32)
        ones_row = sb("ones_row", [1, NS])
        ring = sb("ring", [P, 2, GC, SLOTS, 2 * F])
        kvs = ring[:, :, :, :, :].rearrange("p a c g f -> p (a c g) f")[:, 0:NB, :]
        logit = sb("logit", [P, 2, GC, SLOTS * H])
        by_slot = sb("by_slot", [P, SLOTS, ROWS])
        dstT = sb("dstT", [ROWS, 2, GE], I32)
        nodst = sb("nodst", [H, GE - TAILE], I32)
        src_idx = sb("src_idx", [P, 2, GC * SLOTS], I32)
        dl_a = sb("dl_a", [P, 2, SLOTS], BF16)
        x_flat = xs[:, :, :].rearrange("p b f -> p (b f)")
        hot_a, hotT = (x_flat[:, n * GE:(n + 1) * GE].bitcast(BF16).rearrange("p (u s n) -> p u s n", u=2, s=SLOTS)
                       for n in range(2))
        prod = x_flat[:, 2 * GE:3 * GE].rearrange("p (u f) -> p u f", u=2)
        part = sb("part", [P, 2, SLOTS * H])
        scratch = work[0:ROWS, :, :].rearrange("p b f -> p (b f)")
        scratch2 = nodes[0:ROWS, :, :].rearrange("p b f -> p (b f)")
        differs, reset, lgT = scratch[:, 0:GE + 1], scratch[:, GE + 1:2 * GE + 2], scratch[:, 2 * GE + 2:3 * GE + 2]
        premax, runmax, lastmax = (scratch2[:, n * GE:(n + 1) * GE] for n in range(3))
        wT = lgT
        W = sb("W", [P, GC, SLOTS, WW])
        dl_c = sb("dl_c", [P, 2, SLOTS])
        hot_c = sb("hot_c", [P, 2, SLOTS, P])
        absent = sb("absent", [P, 2, H])
        stepmax = sb("stepmax", [P, 2, H])
        newmax = sb("newmax", [P, 2, H])
        delta = sb("delta", [P, 2, 2 * H])
        factor = sb("factor", [P, 2, 2 * H])
        oldpart = sb("oldpart", [P, 2, AW])
        newpart = sb("newpart", [P, 2, AW])
        node_max = sb("node_max", [P, NB, H])
        node_sum = sb("node_sum", [P, NB, AW])
        rden = sb("rden", [P, NB, H])
        res = work

        pT = [ps(f"pT{u}", [P, SLOTS, P], BF16) for u in range(2)]
        pQ = [ps(f"pQ{u}", [P, 512]) for u in range(2)]
        pL = ps("pL", [P, 2, 512])
        pW = [ps(f"pW{u}", [P, 512]) for u in range(2)]

        s_const = sem("const_loaded")
        s_const2 = sem("steps_loaded")
        s_x = sem("x_loaded")
        s_idx = sem("indices_loaded")
        s_pad = sem("pads_cleared")
        s_bf = sem("constants_made")
        s_mk, s_iota, s_ident, s_acc = sem("ident_cleared"), sem("iota_made"), sem("ident_made"), sem("sums_cleared")
        s_bys = sem("logits_by_slot")
        s_tick = sem("pe_tick")
        s_src = [sem(f"indices_loaded{u}") for u in range(2)]
        s_tail, s_part_all = sem("tail_loaded"), sem("logits_finished")
        s_var, s_sqrt = sem("variance_ready"), sem("root_ready")
        s_merged = sem("superchunk_merged")
        s_tab = sem("table_chain")
        s_tabw = sem("table_written")
        s_steps = sem("steps_ready")
        s_ln = sem("layernorm_chain")
        s_lnready = sem("nodes_normalised")
        s_nT = sem("node_transposed")
        s_nTc = sem("node_transpose_copied")
        s_qkv = sem("qkv_done")
        s_kvc = sem("kv_copied")
        s_qc = sem("q_copied")
        s_kvw = sem("kv_written")
        s_qs = sem("q_split_chain")
        s_qready = sem("q_parts_ready")
        s_gather = sem("superchunk_gather_begun")
        s_slot = [sem(f"gathered{c}") for c in range(2 * GC)]
        s_landed = sem("groups_landed")
        s_edge = [sem(f"edge_data_loaded{u}") for u in range(2)]
        s_dla, s_ra, s_tr, s_rt, s_qx = sem("dl_a_done"), sem("hot_a_ready"), sem("hot_transposed"), sem("hotT_ready"), sem("q_expanded")
        s_prod, s_part, s_lg = sem("product_done"), sem("partial_logits"), sem("logits_added")
        s_lt, s_ltc, s_mask, s_scan, s_sub, s_exp = sem("logits_transposed"), sem("lgT_ready"), sem("mask_chain"), sem("scan_chain"), sem("shifted"), sem("weights_exp")
        s_lm, s_bt, s_btc, s_w = sem("lastmax_ready"), sem("weights_transposed"), sem("weights_copied"), sem("values_weighted")
        s_dlc, s_rc, s_agg, s_mg = sem("dl_c_done"), sem("hot_c_ready"), sem("aggregated"), sem("merged")
        s_mc, s_dd, s_ef, s_m2 = sem("merge_chain"), sem("delta_ready"), sem("factor_ready"), sem("merge_sum_chain")
        s_fin, s_finn = sem("final_chain"), sem("sums_normalised")
        s_oT, s_oTc, s_om, s_or = sem("sum_transposed"), sem("sum_transpose_copied"), sem("projected"), sem("result_ready")
        s_out = sem("out_written")

        block = ctx.enter_context(nc.Block())

        def sc_bounds(eng, sc):
            lo = eng.value_load(begin[0:1, bass.ds(sc, 1)], min_val=0, max_val=NS * MAXPAIRS)
            n = eng.value_load(pairs[0:1, bass.ds(sc, 1)], min_val=0, max_val=MAXPAIRS)
            return lo, n

        def step_group(eng, k):
            return eng.value_load(steps[0:1, bass.ds(k, 1)], min_val=0, max_val=GC - 1)

        def step_block(eng, k, first, g):
            return nc.s_assert_within(k + first - g, 0, NB - 1,
                                      skip_runtime_bounds_check_because="a superchunk ends at most 3 steps past the last block")

        def sc_block(eng, sc):
            return eng.value_load(first_row[0:1, bass.ds(sc, 1)], min_val=0, max_val=NB - 1)

        def edge_count(j, v):
            return (j + 1) * 16 * (GC + 1)

        @block.sync
        def _(sp):
            sp.dma_start(xs[:, 0:FULLB, :], x[0:FULLB * P, :].rearrange("(b p) f -> p b f", p=P)).then_inc(s_x, 16)
            with nc.allow_non_contiguous_dma(reason="single words, a few hundred in all"):
                sp.dma_start(last_dst[0:NS - 1, :], dst[0:(NS - 1) * SE].rearrange("(s c e) -> s c e", s=NS - 1, c=GC)
                             [:, :, GE - 1]).then_inc(s_const, 16)
                sp.dma_start(last_dst[NS - 1:NS, 0:GC - 1], dst[(NS - 1) * SE:(NG - 1) * GE].rearrange("(s c e) -> s c e", s=1, c=GC - 1)
                             [:, :, GE - 1]).then_inc(s_const, 16)
                sp.dma_start(last_dst[NS - 1:NS, GC - 1:GC], dst[E - 1:E].rearrange("(a b) -> a b", a=1)).then_inc(s_const, 16)
                sp.dma_start(first_dst[0:NS - 1, :], dst[0:(NS - 1) * SE].rearrange("(s e) -> s e", s=NS - 1)
                             [:, 0:1]).then_inc(s_const, 16)
                sp.dma_start(first_dst[NS - 1:NS, :], dst[(NS - 1) * SE:(NS - 1) * SE + 1].rearrange("(s e) -> s e", s=1)).then_inc(s_const, 16)
            for n, (w, b) in enumerate(((Wq, bq), (Wk, bk), (Wv, bv))):
                sp.dma_start(wqkv[0:F, n * F:(n + 1) * F], w).then_inc(s_const, 16)
                sp.dma_start(wqkv[F:F + 1, n * F:(n + 1) * F], b.rearrange("(a f) -> a f", a=1)).then_inc(s_const, 16)
            sp.dma_start(wo[0:F, :], Wo).then_inc(s_const, 16)
            sp.dma_start(wo[F:F + 1, :], bo.rearrange("(a f) -> a f", a=1)).then_inc(s_const, 16)
            sp.wait_ge(s_pad, 1)
            sp.dma_start(xs[0:TAILN, FULLB, :], x[FULLB * P:N, :]).then_inc(s_x, 16)
            sp.dma_start(dst_i[:, 0:(NG - 1) * SLOTS].rearrange("p (c g) -> p c g", g=SLOTS),
                         dst[0:(NG - 1) * GE].rearrange("(c p g) -> p c g", p=P, g=SLOTS)).then_inc(s_idx, 16)
            sp.dma_start(dst_i[0:TAILP, (NG - 1) * SLOTS:NG * SLOTS],
                         dst[(NG - 1) * GE:E].rearrange("(p g) -> p g", g=SLOTS)).then_inc(s_idx, 16)
            sp.wait_ge(s_steps, 1)
            sp.dma_start(group_dram, tab_g[:, :]).then_inc(s_tabw, 16)
            sp.dma_start(base_dram, tab[:, 1, :]).then_inc(s_tabw, 16)
            with nc.allow_non_contiguous_dma(reason="single words, 56 in all"):
                sp.dma_start(meta_dram.rearrange("m s -> s m"), meta[:, :]).then_inc(s_tabw, 16)
            sp.wait_ge(s_tabw, 48)
            sp.dma_start(base128[:, :], base_dram.rearrange("(a s) k -> a (s k)", a=1).to_broadcast([P, NS * KT])).then_inc(s_const2, 16)
            sp.dma_start(steps[:, :], group_dram.rearrange("(a s) k -> a (s k)", a=1)).then_inc(s_const2, 16)
            sp.dma_start(meta_row[:, :, :], meta_dram.rearrange("(a m) s -> a m s", a=1)).then_inc(s_const2, 16)
            for c in range(NCH):
                sp.wait_ge(s_kvc, CH * (c + 1))
                sp.dma_start(kv_dram[c * CH * P:(c + 1) * CH * P, :].rearrange("(b p) f -> p b f", p=P),
                             kvs[:, c * CH:(c + 1) * CH, :]).then_inc(s_kvw, 16)

            def edge_data(sc, u, full=GC):
                sp.dma_start(logit[:, u, 0:full, :],
                             attr[bass.ds(sc * SE, full * GE), :].rearrange("(c p g) h -> p c (g h)", p=P, g=SLOTS)
                             ).then_inc(s_edge[u], 16)
                for c in range(full):
                    sp.dma_start(dstT[c * H:(c + 1) * H, u, :],
                                 dst[bass.ds(sc * SE + c * GE, GE)].rearrange("(a e) -> a e", a=1).to_broadcast([H, GE])
                                 ).then_inc(s_edge[u], 16)

            def indices(sc, u, full=GC):
                sp.dma_start(src_idx[:, u, 0:full * SLOTS].rearrange("p (c g) -> p c g", g=SLOTS),
                             src[bass.ds(sc * SE, full * GE)].rearrange("(c p g) -> p c g", p=P, g=SLOTS)
                             ).then_inc(s_src[u], 16)

            def landed(times, u):
                for c in range(GC):
                    sp.wait_ge(s_slot[u * GC + c], times * 16 * SLOTS)
                    sp.sem_inc(s_landed, 1)

            sp.wait_ge(s_pad, 2)
            indices(0, 0)
            indices(1, 1)
            edge_data(0, 0)
            with sp.Fori(0, NS // 2 - 2) as j:
                for u in range(2):
                    landed(j + 1, u)
                    sp.wait_ge(s_w, j * 2 + u + 1)
                    indices(j * 2 + u + 2, u)
                    edge_data(j * 2 + u + 1, 1 - u)
            landed(NS // 2 - 1, 0)
            sp.wait_ge(s_w, NS - 3)
            indices(NS - 2, 0)
            edge_data(NS - 3, 1)
            landed(NS // 2 - 1, 1)
            sp.wait_ge(s_w, NS - 2)
            sp.dma_start(src_idx[0:TAILP, 1, (GC - 1) * SLOTS:], src[(NG - 1) * GE:E].rearrange("(p g) -> p g", g=SLOTS)
                         ).then_inc(s_tail, 16)
            sp.wait_ge(s_tail, 16)
            indices(NS - 1, 1, full=GC - 1)
            edge_data(NS - 2, 0)
            landed(NS // 2, 0)
            sp.wait_ge(s_w, NS - 1)
            sp.dma_start(logit[0:TAILP, 1, GC - 1, :],
                         attr[(NG - 1) * GE:E, :].rearrange("(p g) h -> p (g h)", g=SLOTS)).then_inc(s_tail, 16)
            sp.dma_start(dstT[(GC - 1) * H:ROWS, 1, 0:TAILE],
                         dst[(NG - 1) * GE:E].rearrange("(a e) -> a e", a=1).to_broadcast([H, TAILE])).then_inc(s_tail, 16)
            sp.wait_ge(s_tail, 48)
            edge_data(NS - 1, 1, full=GC - 1)
            sp.dma_start(dstT[(GC - 1) * H:ROWS, 1, TAILE:GE], nodst[:, :]).then_inc(s_edge[1], 16)
            landed(NS // 2, 1)
            sp.wait_ge(s_w, NS)
            sp.wait_ge(s_part_all, 1)
            sp.dma_start(xs[:, 0:FULLB, :], x[0:FULLB * P, :].rearrange("(b p) f -> p b f", p=P)).then_inc(s_x, 16)
            sp.dma_start(xs[0:TAILN, FULLB, :], x[FULLB * P:N, :]).then_inc(s_x, 16)
            for c in range(NCH):
                sp.wait_ge(s_or, CH * (c + 1))
                hi = min((c + 1) * CH, FULLB)
                sp.dma_start(out[c * CH * P:hi * P, :].rearrange("(b p) f -> p b f", p=P),
                             res[:, c * CH:hi, :]).then_inc(s_out, 16)
            sp.dma_start(out[FULLB * P:N, :], res[0:TAILN, FULLB, :]).then_inc(s_out, 16)
            sp.wait_ge(s_out, 16 * (NCH + 1))

        @block.gpsimd
        def _(pool):
            pool.memset(ident[:, :], 0.0).then_inc(s_mk, 1)
            pool.iota(iota_i[:, :], pattern=[[1, P]], base=0, channel_multiplier=0).then_inc(s_iota, 1)
            pool.wait_ge(s_mk, 1)
            pool.affine_select(out=ident[:, :], in_=ident[:, :], compare_op=ALU.not_equal, fill=1.0,
                               base=0, pattern=[[-1, P]], channel_multiplier=1).then_inc(s_ident, 1)
            pool.memset(node_sum[:, :, :], 0.0).then_inc(s_acc, 1)
            pool.memset(node_max[:, :, :], -BIG).then_inc(s_acc, 1)
            pool.wait_ge(s_kvw, 16 * NCH)

            def gather(j, u):
                pool.wait_ge(s_src[u], (j + 1) * 16)
                pool.sem_inc(s_gather, 1)
                for c in range(GC):
                    for g in range(SLOTS):
                        col = c * SLOTS + g
                        pool.indirect_dma_start(ring[:, u, c, g, :], None, kv_dram,
                                                bass.IndirectOffsetOnAxis(ap=src_idx[:, u, col:col + 1], axis=0)
                                                ).then_inc(s_slot[u * GC + c], 16)

            with pool.Fori(0, NS // 2) as j:
                for u in range(2):
                    gather(j, u)

        def qkv(pe, b):
            pe.wait_ge(s_nTc, b + 1)
            if b >= 2:
                pe.wait_ge(s_qc, b - 1)
            pe.matmul(pQ[b % 2][:, 0:3 * F], nodesT[:, b % 2, :], wqkv[:, :], start=True, stop=True).then_inc(s_qkv, 1)

        def project(pe, b):
            pe.wait_ge(s_oTc, b + 1)
            if b >= 2:
                pe.wait_ge(s_or, b - 1)
            pe.matmul(pQ[b % 2][:, 0:F], nodesT[:, b % 2, :], wo[:, :], start=True, stop=True).then_inc(s_om, 1)

        def transposes(pe, r):
            for u in range(2):
                pe.wait_ge(s_ra, r * 2 + u + 3)
                pe.wait_ge(s_rt, r * 2 + u + 1)
                for g in range(SLOTS):
                    mm = pe.transpose(pT[u][:, g, :], hot_a[:, u, g, :], ident_bf[:, :])
                mm.then_inc(s_tr, 1)

        @block.tensor
        def _(pe):
            pe.sem_inc(s_tr, 2)
            pe.sem_inc(s_qx, 2)
            pe.sem_inc(s_agg, 2)
            pe.wait_ge(s_const, 16 * 13)
            pe.wait_ge(s_ident, 1)
            pe.wait_ge(s_bf, 3)
            for b in range(NB):
                u = b % 2
                if b % CH == 0:
                    pe.wait_ge(s_lnready, b // CH + 1)
                if b >= 2:
                    pe.wait_ge(s_nTc, b - 1)
                pe.transpose(pW[u][0:F, 0:P], nodes[:, b, :], ident[:, :]).then_inc(s_nT, 1)
                if b >= 1:
                    qkv(pe, b - 1)
            qkv(pe, NB - 1)

            pe.wait_ge(s_qready, 1)
            pe.wait_ge(s_steps, 2)
            with pe.Fori(0, NS // 2) as j:
                for v in range(2):
                    sc = j * 2 + v
                    lo, cnt = sc_bounds(pe, sc)
                    first = sc_block(pe, sc)
                    transposes(pe, lo + sc)
                    with pe.Fori(0, cnt) as l:
                        i = lo + l
                        transposes(pe, i + sc + 1)
                        k = l * 2 + sc * KT
                        for u in range(2):
                            b = step_block(pe, l * 2 + u, first, step_group(pe, k + u))
                            pe.wait_ge(s_rt, (i + sc) * 2 + u + 3)
                            pe.wait_ge(s_prod, i * 2 + u + 1)
                            for g in range(SLOTS):
                                for n in range(3):
                                    mm = pe.matmul(pQ[u][:, g * F:(g + 1) * F], hotT[:, u, g, :],
                                                   q_parts[:, n, bass.ds(b, 1), :].rearrange("p a f -> p (a f)"),
                                                   start=(n == 0), stop=(n == 2))
                            mm.then_inc(s_qx, 1)
                    pe.wait_ge(s_bys, sc + 1)
                    pe.sem_inc(s_tick, 1)
                    for g in range(SLOTS):
                        mm = pe.transpose(pL[0:ROWS, g // 4, (g % 4) * P:(g % 4 + 1) * P],
                                          by_slot[:, g, :], ident[:, :])
                    mm.then_inc(s_lt, 1)
                    for n, rows in enumerate((wT, lastmax)):
                        pe.wait_ge(s_exp if n == 0 else s_lm, sc + 1)
                        pe.sem_inc(s_tick, 1)
                        for g in range(SLOTS):
                            mm = pe.transpose(pW[n][:, g * ROWS:(g + 1) * ROWS],
                                              rows[:, :].rearrange("r (p g) -> r g p", g=SLOTS)[:, g, :], ident[0:ROWS, 0:ROWS])
                        mm.then_inc(s_bt, 1)
                    pe.wait_ge(s_w, sc + 1)
                    pe.sem_inc(s_tick, 1)
                    with pe.Fori(0, cnt) as l:
                        i = lo + l
                        k = l * 2 + sc * KT
                        for u in range(2):
                            c = step_group(pe, k + u)
                            pe.wait_ge(s_rc, (i + sc) * 2 + u + 3)
                            pe.wait_ge(s_mg, i * 2 + u + 1)
                            for g in range(SLOTS):
                                mm = pe.matmul(pW[u][:, 0:WW], hot_c[:, u, g, :],
                                               W[:, bass.ds(c, 1), g, :].rearrange("p a w -> p (a w)"),
                                               start=(g == 0), stop=(g == SLOTS - 1))
                            mm.then_inc(s_agg, 1)

            for b in range(NB):
                u = b % 2
                if b == 0:
                    pe.wait_ge(s_finn, 1)
                if b >= 2:
                    pe.wait_ge(s_oTc, b - 1)
                pe.transpose(pW[u][0:F, 0:P], nodes[:, b, :], ident[:, :]).then_inc(s_oT, 1)
                if b >= 1:
                    project(pe, b - 1)
            project(pe, NB - 1)

        @block.scalar
        def _(act):
            act.sem_inc(s_rt, 2)
            act.wait_ge(s_var, 1)
            act.activation(stat[:, 2, :], stat[:, 1, :], ACT.Sqrt).then_inc(s_sqrt, 1)
            for b in range(NB):
                u = b % 2
                act.wait_ge(s_nT, b + 1)
                if b >= 2:
                    act.wait_ge(s_qkv, b - 1)
                if b < 2:
                    act.wait_ge(s_bf, 3)
                act.copy(nodesT[0:F, u, :], pW[u][0:F, 0:P]).then_inc(s_nTc, 1)
                if b >= 1:
                    act.wait_ge(s_qkv, b)
                    act.copy(kvs[:, b - 1, :], pQ[(b - 1) % 2][:, F:3 * F]).then_inc(s_kvc, 1)
            act.wait_ge(s_qkv, NB)
            act.copy(kvs[:, NB - 1, :], pQ[(NB - 1) % 2][:, F:3 * F]).then_inc(s_kvc, 1)
            act.wait_ge(s_steps, 2)

            with act.Fori(0, NS // 2) as j:
                for v in range(2):
                    sc = j * 2 + v
                    lo, cnt = sc_bounds(act, sc)
                    with act.Fori(0, cnt + 1) as l:
                        i = lo + l
                        for u in range(2):
                            act.wait_ge(s_tr, (i + sc) * 2 + u + 3)
                            act.wait_ge(s_qx, i * 2 + u + 1)
                            act.copy(hotT[:, u, :, :], pT[u][:, :, :]).then_inc(s_rt, 1)
                    act.wait_ge(s_lg, (lo + cnt) * 2 + 2)
                    act.copy(by_slot[:, :, :].rearrange("p g (c h) -> p g c h", h=H),
                             logit[:, v, :, :].rearrange("p c (g h) -> p g c h", g=SLOTS)).then_inc(s_bys, 1)
                    act.wait_ge(s_lt, sc + 1)
                    act.copy(lgT[:, :].rearrange("r (p g) -> r g p", g=SLOTS),
                             pL[0:ROWS, :, :].rearrange("r a (b p) -> r (a b) p", p=P)).then_inc(s_ltc, 1)
                    act.wait_ge(s_sub, sc + 1)
                    act.activation(wT[:, :], premax[:, :], ACT.Exp).then_inc(s_exp, 1)
                    for n in range(2):
                        act.wait_ge(s_bt, sc * 2 + n + 1)
                        dest = W[:, :, :, D:AW:D + 1] if n == 0 else W[:, :, :, AW:WW]
                        act.copy(dest.rearrange("p c g h -> p g c h"),
                                 pW[n][:, 0:SLOTS * ROWS].rearrange("p (g c h) -> p g c h", g=SLOTS, c=GC)).then_inc(s_btc, 1)
                    with act.Fori(0, cnt) as l:
                        i = lo + l
                        for u in range(2):
                            act.wait_ge(s_dd, i * 2 + u + 1)
                            act.activation(factor[:, u, :], delta[:, u, :], ACT.Exp).then_inc(s_ef, 1)

            for b in range(NB):
                u = b % 2
                act.wait_ge(s_oT, b + 1)
                if b >= 2:
                    act.wait_ge(s_om, b - 1)
                act.copy(nodesT[0:F, u, :], pW[u][0:F, 0:P]).then_inc(s_oTc, 1)

        @block.vector
        def _(dve):
            for s in (s_ra, s_rc, s_prod, s_part, s_lg, s_mg):
                dve.sem_inc(s, 2)
            links = [0]

            def link(ins):
                links[0] += 1
                ins.then_inc(s_ln, 1)
                dve.wait_ge(s_ln, links[0])

            dve.memset(xs[:, FULLB:NB, :], 0.0)
            dve.memset(nodst[:, :], NODST)
            dve.memset(dst_i[:, (NG - 1) * SLOTS:], NODST)
            dve.memset(nodesT[F:F + 1, :, :], 1.0)
            dve.memset(ones_row[:, :], 1.0)
            dve.memset(begin_f[:, :], 0.0).then_inc(s_pad, 2)
            dve.wait_ge(s_iota, 1)
            dve.tensor_copy(iota[:, :], iota_i[:, :]).then_inc(s_bf, 1)
            dve.tensor_copy(iota_bf[:, :], iota_i[:, :]).then_inc(s_bf, 1)
            dve.wait_ge(s_ident, 1)
            dve.tensor_copy(ident_bf[:, :], ident[:, :]).then_inc(s_bf, 1)

            dve.wait_ge(s_const, 16 * 13)
            dve.wait_ge(s_bf, 3)
            dve.tensor_scalar(last_blk[:, :], last_dst[:, :], 7, None, ALU.arith_shift_right)
            link(dve.tensor_scalar(first_blk[:, :], first_dst[:, :], 7, None, ALU.arith_shift_right))
            dve.tensor_copy(first_f[:, :], first_blk[:, :])
            link(dve.tensor_tensor(last_step[:, :], last_blk[:, :], iota[0:NS, 0:GC], ALU.add))
            link(dve.tensor_scalar(last_step[:, :], last_step[:, :], first_f[:, 0:1], None, ALU.subtract))
            link(dve.tensor_tensor(reach[:, :, :], last_step[:, None, :].to_broadcast([NS, KT, GC]),
                                   iota[0:NS, 0:KT, None].to_broadcast([NS, KT, GC]), ALU.is_lt))
            link(dve.tensor_reduce(tab[:, 0, :], reach[:, :, :], AX_X, ALU.add))
            link(dve.tensor_scalar(tab[:, 0, :], tab[:, 0, :], float(GC - 1), None, ALU.min))
            dve.tensor_copy(tab_g[:, :], tab[:, 0, :])
            link(dve.scalar_tensor_tensor(out=tab[:, 1, :], in0=iota[0:NS, 0:KT], scalar=first_f[:, 0:1],
                                          in1=tab[:, 0, :], op0=ALU.add, op1=ALU.subtract))
            link(dve.tensor_scalar(tab[:, 1, :], tab[:, 1, :], float(P), None, ALU.mult))
            link(dve.tensor_scalar(iti[:, 0:1], last_step[:, GC - 1:GC], 2.0, None, ALU.add))
            link(dve.tensor_scalar(iti[:, 1:2], iti[:, 0:1], 1, None, ALU.arith_shift_right))
            dve.tensor_copy(meta[:, 0:1], iti[:, 1:2])
            dve.tensor_copy(meta[:, 1:2], first_f[:, :]).then_inc(s_steps, 1)

            dve.wait_ge(s_x, 32)
            link(dve.tensor_reduce(stat[:, 0, :], xs[:, :, :], AX_X, ALU.add))
            link(dve.tensor_scalar(stat[:, 0, :], stat[:, 0, :], 1.0 / F, None, ALU.mult))
            link(dve.tensor_tensor(nodes[:, :, :], xs[:, :, :], stat[:, 0, :, None].to_broadcast([P, NB, F]), ALU.subtract))
            link(dve.tensor_tensor(work[:, :, :], nodes[:, :, :], nodes[:, :, :], ALU.mult))
            link(dve.tensor_reduce(stat[:, 1, :], work[:, :, :], AX_X, ALU.add))
            dve.tensor_scalar(stat[:, 1, :], stat[:, 1, :], 1.0 / F, 1e-5, ALU.mult, ALU.add).then_inc(s_var, 1)
            dve.wait_ge(s_sqrt, 1)
            link(dve.reciprocal(stat[:, 3, :], stat[:, 2, :]))
            for c in range(NCH):
                part_c = slice(c * CH, (c + 1) * CH)
                dve.scalar_tensor_tensor(out=nodes[:, part_c, :], in0=nodes[:, part_c, :], scalar=0.0,
                                         in1=stat[:, 3, part_c, None].to_broadcast([P, CH, F]),
                                         op0=ALU.max, op1=ALU.mult).then_inc(s_lnready, 1)
            for b in range(NB):
                dve.wait_ge(s_kvc, b + 1)
                dve.tensor_scalar(work[:, b, :], pQ[b % 2][:, 0:F], SCALE, None, ALU.mult).then_inc(s_qc, 1)
            dve.wait_ge(s_qc, NB)
            link(dve.tensor_copy(q_parts[:, 0, :, :], work[:, :, :]))
            link(dve.tensor_tensor(work[:, :, :], work[:, :, :], q_parts[:, 0, :, :], ALU.subtract))
            link(dve.tensor_copy(q_parts[:, 1, :, :], work[:, :, :]))
            dve.tensor_tensor(q_parts[:, 2, :, :], work[:, :, :], q_parts[:, 1, :, :], ALU.subtract).then_inc(s_qready, 1)
            dve.wait_ge(s_const2, 48)
            dve.tensor_copy(first_row[:, :], meta_row[:, 1, :])
            dve.tensor_copy(pairs[:, :], meta_row[:, 0, :])
            link(dve.tensor_tensor_scan(begin_f[:, 1:], ones_row[:, :], meta_row[:, 0, :], 0.0, ALU.mult, ALU.add))
            dve.tensor_copy(begin[:, :], begin_f[:, :]).then_inc(s_steps, 1)
            dve.wait_ge(s_steps, 2)
            dve.wait_ge(s_acc, 2)
            dve.wait_ge(s_idx, 32)
            dve.wait_ge(s_qready, 1)
            dve.memset(differs[:, 0:1], 1.0)
            link(dve.memset(differs[:, GE:GE + 1], 1.0))

            def onehots(r, k, sc, lg_free, dl, hot, iota_t, s_dl, s_hot, s_users, users):
                for u in range(2):
                    g = step_group(dve, k + u)
                    dve.wait_ge(s_hot, r * 2 + u + 1)
                    dve.tensor_scalar(dl[:, u, :], dst_i[:, bass.ds((g + sc * GC) * SLOTS, SLOTS)],
                                      base128[:, bass.ds(k + u, 1)], None, ALU.subtract).then_inc(s_dl, 1)
                for u in range(2):
                    dve.wait_ge(s_dl, r * 2 + u + 1)
                    dve.wait_ge(s_users, users * 2 + u + 1)
                    dve.tensor_tensor(hot[:, u, :, :], iota_t[:, None, :].to_broadcast([P, SLOTS, P]),
                                      dl[:, u, :, None].to_broadcast([P, SLOTS, P]), ALU.is_equal).then_inc(s_hot, 1)

            def onehots_a(r, k, sc):
                onehots(r, k, sc, None, dl_a, hot_a, iota_bf, s_dla, s_ra, s_tr, r)

            def onehots_c(r, k, sc, i):
                onehots(r, k, sc, None, dl_c, hot_c, iota, s_dlc, s_rc, s_agg, i)

            MC = 6
            MS = 2

            with dve.Fori(0, NS // 2) as j:
                for v in range(2):
                    sc = j * 2 + v
                    lo, cnt = sc_bounds(dve, sc)
                    first = sc_block(dve, sc)
                    dve.wait_ge(s_edge[v], edge_count(j, v))
                    onehots_a(lo + sc, sc * KT, sc)
                    with dve.Fori(0, cnt) as l:
                        i = lo + l
                        k = l * 2 + sc * KT
                        onehots_a(i + sc + 1, k + 2, sc)
                        for u in range(2):
                            g = step_group(dve, k + u)
                            dve.wait_ge(s_qx, i * 2 + u + 3)
                            dve.wait_ge(s_part, i * 2 + u + 1)
                            dve.wait_ge(s_landed, g + sc * GC + 1)
                            kk = ring[:, v, bass.ds(g, 1), :, 0:F].rearrange("p a s f -> p (a s) f")
                            dve.tensor_tensor(prod[:, u, :].rearrange("p (s f) -> p s f", f=F),
                                              pQ[u][:, :].rearrange("p (s f) -> p s f", f=F), kk, ALU.mult).then_inc(s_prod, 1)
                        for u in range(2):
                            dve.wait_ge(s_prod, i * 2 + u + 3)
                            dve.wait_ge(s_lg, i * 2 + u + 1)
                            dve.tensor_reduce(part[:, u, :], prod[:, u, :].rearrange("p (a d) -> p a d", d=D),
                                              AX_X, ALU.add).then_inc(s_part, 1)
                        for u in range(2):
                            g = step_group(dve, k + u)
                            lg = logit[:, v, bass.ds(g, 1), :].rearrange("p a w -> p (a w)")
                            dve.wait_ge(s_part, i * 2 + u + 3)
                            dve.wait_ge(s_lg, i * 2 + u + 2)
                            dve.tensor_tensor(lg, lg, part[:, u, :], ALU.add).then_inc(s_lg, 1)
                    dve.tensor_tensor(differs[:, 1:GE], dstT[:, v, 1:GE], dstT[:, v, 0:GE - 1], ALU.not_equal).then_inc(s_mask, 1)
                    dve.wait_ge(s_mask, sc * 2 + 1)
                    dve.tensor_scalar(reset[:, :], differs[:, :], -BIG, None, ALU.mult).then_inc(s_mask, 1)
                    dve.wait_ge(s_mask, sc * 2 + 2)
                    dve.wait_ge(s_ltc, sc + 1)
                    dve.tensor_tensor_scan(premax[:, :], reset[:, 0:GE], lgT[:, :], -BIG, ALU.add, ALU.max).then_inc(s_scan, 1)
                    dve.wait_ge(s_scan, sc * 2 + 1)
                    dve.tensor_tensor_scan(runmax[:, ::-1], reset[:, 1:][:, ::-1], premax[:, ::-1], -BIG,
                                           ALU.add, ALU.max).then_inc(s_scan, 1)
                    dve.wait_ge(s_scan, sc * 2 + 2)
                    dve.tensor_tensor(premax[:, :], lgT[:, :], runmax[:, :], ALU.subtract).then_inc(s_sub, 1)
                    dve.tensor_tensor(lastmax[:, :], runmax[:, :], differs[:, 1:], ALU.mult).then_inc(s_lm, 1)
                    onehots_c(lo + sc, sc * KT, sc, lo)
                    dve.wait_ge(s_btc, sc * 2 + 2)
                    for c in range(GC):
                        ins = dve.tensor_tensor(W[:, c, :, 0:AW].rearrange("p s (h e) -> p s h e", e=D + 1)[:, :, :, 0:D],
                                                ring[:, v, c, :, F:2 * F].rearrange("p s (h d) -> p s h d", d=D),
                                                W[:, c, :, D:AW:D + 1][:, :, :, None].to_broadcast([P, SLOTS, H, D]), ALU.mult)
                    ins.then_inc(s_w, 1)
                    with dve.Fori(0, cnt) as l:
                        i = lo + l
                        k = l * 2 + sc * KT
                        onehots_c(i + sc + 1, k + 2, sc, i + 1)
                        blocks = []
                        for u in range(2):
                            b = step_block(dve, l * 2 + u, first, step_group(dve, k + u))
                            blocks.append(b)
                            t = i * 2 + u
                            mold = node_max[:, bass.ds(b, 1), :].rearrange("p a h -> p (a h)")
                            dve.wait_ge(s_agg, t + 3)
                            dve.tensor_scalar(absent[:, u, :], pW[u][:, D:AW:D + 1], 0.5, -BIG, ALU.is_lt, ALU.mult).then_inc(s_mc, 1)
                            dve.wait_ge(s_mc, t * MC + 1)
                            dve.tensor_tensor(stepmax[:, u, :], absent[:, u, :], pW[u][:, AW:WW], ALU.add).then_inc(s_mc, 1)
                            dve.wait_ge(s_mc, t * MC + 2)
                            dve.tensor_tensor(newmax[:, u, :], stepmax[:, u, :], mold, ALU.max).then_inc(s_mc, 1)
                            dve.wait_ge(s_mc, t * MC + 3)
                            dve.tensor_tensor(delta[:, u, 0:H], mold, newmax[:, u, :], ALU.subtract).then_inc(s_mc, 1)
                            dve.tensor_tensor(delta[:, u, H:2 * H], stepmax[:, u, :], newmax[:, u, :], ALU.subtract).then_inc(s_dd, 1)
                            dve.wait_ge(s_mc, t * MC + 4)
                            dve.tensor_tensor(mold, mold, stepmax[:, u, :], ALU.max).then_inc(s_mc, 1)
                            dve.wait_ge(s_mc, t * MC + 5)
                            dve.sem_inc(s_mc, 1)
                        for u in range(2):
                            t = i * 2 + u
                            acc = node_sum[:, bass.ds(blocks[u], 1), :].rearrange("p a (h e) -> p (a h) e", e=D + 1)
                            old = oldpart[:, u, :].rearrange("p (h e) -> p h e", e=D + 1)
                            new = newpart[:, u, :].rearrange("p (h e) -> p h e", e=D + 1)
                            dve.wait_ge(s_ef, t + 1)
                            dve.tensor_tensor(old, acc, factor[:, u, 0:H, None].to_broadcast([P, H, D + 1]), ALU.mult).then_inc(s_m2, 1)
                            dve.tensor_tensor(new, pW[u][:, 0:AW].rearrange("p (h e) -> p h e", e=D + 1),
                                              factor[:, u, H:2 * H, None].to_broadcast([P, H, D + 1]), ALU.mult).then_inc(s_m2, 1)
                            dve.wait_ge(s_m2, t * MS + 2)
                            dve.tensor_tensor(acc, old, new, ALU.add).then_inc(s_mg, 1)
                            dve.wait_ge(s_mg, t + 3)

            dve.sem_inc(s_part_all, 1)
            fl = [0]

            def flink(ins):
                fl[0] += 1
                ins.then_inc(s_fin, 1)
                dve.wait_ge(s_fin, fl[0])

            acc = node_sum[:, :, :].rearrange("p b (h e) -> p b h e", e=D + 1)
            flink(dve.tensor_scalar(rden[:, :, :], acc[:, :, :, D], 1e-16, None, ALU.add))
            flink(dve.reciprocal(rden[:, :, :], rden[:, :, :]))
            dve.tensor_tensor(nodes[:, :, :].rearrange("p b (h d) -> p b h d", d=D), acc[:, :, :, 0:D],
                              rden[:, :, :, None].to_broadcast([P, NB, H, D]), ALU.mult).then_inc(s_finn, 1)
            dve.wait_ge(s_x, 64)
            for b in range(NB):
                dve.wait_ge(s_om, b + 1)
                dve.tensor_tensor(res[:, b, :], pQ[b % 2][:, 0:F], xs[:, b, :], ALU.add).then_inc(s_or, 1)


_INS = ["x", "src", "dst", "edge_attr_8", "L0_gnn_Wq", "L0_gnn_bq", "L0_gnn_Wk", "L0_gnn_bk", "L0_gnn_Wv", "L0_gnn_bv",
        "L0_gnn_Wo", "L0_gnn_bo"]


def kernel(**inputs):
    import concourse.bacc as bacc
    from concourse.bass_utils import run_bass_kernel_spmd

    nc = bacc.Bacc("TRN2", target_bir_lowering=False, num_devices=1)
    arrays, args = {}, []
    for name in _INS:
        a = np.ascontiguousarray(inputs[name])
        arrays[f"in_{name}"] = a
        args.append(nc.dram_tensor(f"in_{name}", a.shape, mybir.dt.from_np(a.dtype), kind="ExternalInput").ap())
    args.append(nc.dram_tensor("out_x", (N, F), F32, kind="ExternalOutput").ap())
    build(nc, *args)
    r = run_bass_kernel_spmd(nc, [arrays], core_ids=[0])
    return r.results[0]["out_x"]
```
